# Optimizing a Trainium2 kernel written in Bass

```python
import numpy as np
import jax
import jax.numpy as jnp

def _softmax(x, axis=-1):
    return jax.nn.softmax(x, axis=axis)

def _gelu(x):
    return jax.nn.gelu(x, approximate=True)

def _silu(x):
    return jax.nn.silu(x)

def _sigmoid(x):
    return jax.nn.sigmoid(x)

def _layernorm(x, axis=-1, eps=1e-05):
    m = jnp.mean(x, axis=axis, keepdims=True)
    v = jnp.var(x, axis=axis, keepdims=True)
    return (x - m) / jnp.sqrt(v + eps)

def _scatter_add(tgt, idx, src, axis=0):
    return tgt.at[idx].add(src)

def _segment_sum(src, seg, n):
    return jax.ops.segment_sum(src, seg, n)
kernel_name = 'mk_adj_resnorm_d2_adj_r2_101dca'

def setup_inputs(seed: int=0):
    np.random.seed(seed)
    _w = jnp.asarray

    def _rec_inputs():
        import jax
        import jax.numpy as jnp
        _gk = jax.random.key(seed)
        x = -0.0003929 + 0.9999 * jax.random.normal(jax.random.fold_in(_gk, 1), (8, 1024, 256), jnp.float32)
        _a = jax.random.bernoulli(jax.random.fold_in(_gk, 2), 0.015625, (8, 1024, 1024))
        _a = jnp.logical_or(_a, jnp.swapaxes(_a, -1, -2))
        _a = jnp.logical_or(_a, jnp.eye(1024, dtype=bool))
        _af = _a.astype(jnp.float32)
        _af = _af * jax.random.uniform(jax.random.fold_in(_gk, 3), (8, 1024, 1024), jnp.float32, 0.05, 1)
        adj = _af
        return (x, adj)
    x, adj = _rec_inputs()

    def _L0_gnn_setup():
        import jax, jax.numpy as jnp
        import numpy as np
        EPS = 1e-06
        key = jax.random.key(seed)
        k1, k2, k3 = jax.random.split(key, 3)
        B, N, F, O = (8, 2048, 256, 256)
        x = jax.random.normal(k1, (B, N, F), dtype=jnp.float32)
        adj = jax.random.uniform(k2, (B, N, N), dtype=jnp.float32)
        W = jax.random.normal(k3, (O, 2 * F), dtype=jnp.float32) * (1.0 / np.sqrt(2 * F))
        return {'x': x, 'adj': adj, 'W': W}
    _L0_gnn_all = _L0_gnn_setup()
    _L0_gnn_in = {k: v for k, v in _L0_gnn_all.items() if k in ('W',)}
    del _L0_gnn_all

    def _L1_gnn_setup():
        import jax, jax.numpy as jnp
        import numpy as np
        N = 4096
        F = 256
        C = 256
        key = jax.random.key(seed)
        k1, k2, k3 = jax.random.split(key, 3)
        X = jax.random.normal(k1, (1, N, F), dtype=jnp.float32)
        A = jax.random.uniform(k2, (1, N, N), dtype=jnp.float32)
        kernel = jax.random.normal(k3, (F, C), dtype=jnp.float32) * (1.0 / np.sqrt(F))
        bias = jnp.zeros((C,), dtype=jnp.float32)
        return {'X': X, 'A': A, 'kernel': kernel, 'bias': bias}
    _L1_gnn_all = _L1_gnn_setup()
    _L1_gnn_in = {k: v for k, v in _L1_gnn_all.items() if k in ('kernel', 'bias')}
    del _L1_gnn_all
    return {'x': x, 'adj': adj, 'L0_gnn_W': _L0_gnn_in['W'], 'L1_gnn_kernel': _L1_gnn_in['kernel'], 'L1_gnn_bias': _L1_gnn_in['bias']}

def reference(x, adj, L0_gnn_W, L1_gnn_kernel, L1_gnn_bias):
    import jax
    import jax.numpy as jnp

    def _L0_gnn_ref(x, adj, W):
        import jax, jax.numpy as jnp
        import numpy as np
        EPS = 1e-06
        deg = jnp.sum(adj, axis=-1, keepdims=True)
        agg = jnp.einsum('bij,bjf->bif', adj, x) / jnp.maximum(deg, EPS)
        cat = jnp.concatenate([x, agg], axis=2)
        out = jnp.einsum('bnf,of->bno', cat, W)
        return jax.nn.relu(out)

    def _L1_gnn_ref(X, A, kernel, bias):
        import jax, jax.numpy as jnp
        import numpy as np
        N = 4096
        F = 256
        C = 256
        Ah = A + jnp.eye(A.shape[-1], dtype=A.dtype)[None, :, :]
        dh = jax.lax.rsqrt(jnp.sum(Ah, axis=-1))
        An = dh[:, :, None] * Ah * dh[:, None, :]
        out = jnp.einsum('bnm,bmf,fc->bnc', An, X, kernel) + bias
        return jax.nn.relu(out)
    x = _layernorm(x + _L0_gnn_ref(x, adj, L0_gnn_W), axis=-1)
    x = _layernorm(x + _L1_gnn_ref(x, adj, L1_gnn_kernel, L1_gnn_bias), axis=-1)
    return x

_drawn_inputs = setup_inputs


def setup_inputs(seed=0):
    import zlib

    import numpy as np

    out = dict(_drawn_inputs(seed))
    spreads = {'L1_gnn_bias': (0.0, 0.1)}
    factors = {}
    for name, (base, spread) in spreads.items():
        noise = np.random.default_rng([zlib.crc32(name.encode()), seed]).standard_normal(out[name].shape)
        drawn = base * np.exp(spread * noise) if base else spread * noise
        out[name] = jnp.asarray(drawn.astype(out[name].dtype))
    for name, factor in factors.items():
        out[name] = (out[name] * factor).astype(out[name].dtype)
    return out
```

```python
import concourse.bass as bass
from concourse import mybir
from contextlib import ExitStack

F32 = mybir.dt.float32
F32R = mybir.dt.float32r
ALU = mybir.AluOpType
ACT = mybir.ActivationFunctionType

P = 128
B, N, F = 8, 1024, 256
T = N // P
FT = F // P
H = 2
NH = N // H
TH = T // H
CH = 4
JC = T // CH
NB = 4
PL = 6
DEG_EPS = 1e-6
LN_EPS = 1e-5


def gnn_two_layers(nc, adjT, x, xT, w, k, bias, out):
    ctx = ExitStack()
    with ctx:
        def sb(name, shape, dt=F32):
            return ctx.enter_context(nc.sbuf_tensor(name, shape, dt))

        def sem(name):
            return ctx.enter_context(nc.semaphore(name))

        raw = sb("adj_raw", [P, H, T, NH])
        a_hi = sb("adj_hi", [P, H * T * NH], F32R)
        a_lo = sb("adj_lo", [P, H * T * NH], F32R)
        diag = sb("adj_diag", [P, T, P])
        xt_raw = sb("xt_raw", [P, FT, N])
        xt_hi = sb("xt_hi", [P, FT, N], F32R)
        xt_lo = sb("xt_lo", [P, FT, N], F32R)
        g1_hi = sb("g1_hi", [P, FT, NH], F32R)
        g1_lo = sb("g1_lo", [P, FT, NH], F32R)
        x_sb = sb("x_sb", [P, T, F])
        x1 = sb("x1", [P, T, F])
        x1s_hi = sb("x1s_hi", [P, T, F], F32R)
        x1s_lo = sb("x1s_lo", [P, T, F], F32R)
        p1 = sb("p1", [P, T, F])
        z_hi = sb("z_hi", [P, T, F + 2], F32R)
        z_lo = sb("z_lo", [P, T, F], F32R)
        w_hi = sb("w_hi", [P, FT, 2 * F], F32R)
        w_lo = sb("w_lo", [P, FT, 2 * F], F32R)
        k_hi = sb("k_hi", [P, FT, F], F32R)
        k_lo = sb("k_lo", [P, FT, F], F32R)
        bias_sb = sb("bias_sb", [P, F])
        u1 = sb("u1", [P, 2, F])
        ident = sb("ident", [P, 1, P])
        ones = sb("ones", [P, T, 2])
        deg_c = sb("deg_c", [P, 2, 1])
        rdeg = sb("rdeg", [P, 2, 1])
        stats = sb("stats", [P, TH, 6])
        smean = sb("smean", [P, TH])
        dmean = sb("dmean", [P, TH])
        dmean2 = sb("dmean2", [P, TH])
        cv = sb("cv", [P, TH])
        v = sb("rs_value", [P, 2 * TH])
        s = sb("rs_root", [P, 2 * TH])
        r = sb("rs_recip", [P, 2 * TH])
        c = sb("rs_corr", [P, 2 * TH])
        d = sb("rs_sum", [P, 2 * TH])
        dh = sb("dh", [P, H, 2 * TH])
        rstd1 = sb("rstd1", [P, TH])
        nb = sb("nb", [P, TH])

        w_raw = x1[:, 0:2 * FT, :].rearrange("p (f o) c -> p f (o c)", f=FT)
        k_raw = x1[:, 2 * FT:3 * FT, :]

        ring_a = ctx.enter_context(nc.psum_tensor("ring_a", [P, NB, 512], F32))
        ring_b = ctx.enter_context(nc.psum_tensor("ring_b", [P, NB, 512], F32))

        w_loaded, k_loaded, bias_loaded = sem("w_loaded"), sem("k_loaded"), sem("bias_loaded")
        xt_loaded = sem("xt_loaded")
        x_loaded = [sem(f"x_loaded{h}") for h in range(H)]
        raw_loaded = [[sem(f"raw_loaded{h}{i}") for i in range(CH)] for h in range(H)]
        x1_free = [sem(f"x1_free{h}") for h in range(H)]
        ident_zero, ident_done, ones_done = sem("ident_zero"), sem("ident_done"), sem("ones_done")
        w_hi_done, w_lo_done = sem("w_hi_done"), sem("w_lo_done")
        adj_hi_done, adj_lo_done = sem("adj_hi_done"), sem("adj_lo_done")
        diag_ready = sem("diag_ready")
        diag_hi_done, diag_lo_done = sem("diag_hi_done"), sem("diag_lo_done")
        xt_hi_done, xt_lo_done = sem("xt_hi_done"), sem("xt_lo_done")
        z_hi_done, z_lo_done = sem("z_hi_done"), sem("z_lo_done")
        z_ones_done = sem("z_ones_done")
        proj0_done = sem("proj0_done")
        agg_done, agg_read = sem("agg_done"), sem("agg_read")
        deg_clamped, rdeg_done = sem("deg_clamped"), sem("rdeg_done")
        resid0_done = sem("resid0_done")
        stats_done = sem("stats_done")
        dmean_done, dmean2_done = sem("dmean_done"), sem("dmean2_done")
        var_ready = sem("var_ready")
        root_done = sem("root_done")
        recip_done, corr_done, sum_done = sem("recip_done"), sem("corr_done"), sem("sum_done")
        rstd_done, nb_done = sem("rstd_done"), sem("nb_done")
        x1_done = sem("x1_done")
        x1s_hi_done, x1s_lo_done = sem("x1s_hi_done"), sem("x1s_lo_done")
        g_done, g_hi_done = sem("g_done"), sem("g_hi_done")
        g_read = sem("g_read")
        proj1_done = sem("proj1_done")
        proj1_read = sem("proj1_read")
        resid1_done = sem("resid1_done")
        out_done = sem("out_done")

        block = ctx.enter_context(nc.Block())

        def adj_block(t, h, j, i0, n):
            at = (h * T + j) * NH + i0
            return t[:, at:at + n]

        def adj_chunk(t, h, i):
            at = (h * T + i * JC) * NH
            return t[:, at:at + JC * NH]

        def adj_diagonal(t, h):
            step = NH + P
            at = h * T * NH + h * TH * NH
            back = 0 if h == 0 else TH * step - TH * NH
            flat = t[:, at - back:at - back + TH * step]
            return flat.rearrange("p (q m) -> p q m", m=step)[:, :, back:back + P]

        def g_part(hi, h, f):
            if h == 0:
                return (xt_hi if hi else xt_lo)[:, f, 0:NH]
            return (g1_hi if hi else g1_lo)[:, f, :]

        @block.sync
        def _(sp):
            def load_adj(n, h):
                for i in range(CH):
                    sp.dma_start(raw[:, h, i * JC:(i + 1) * JC, :],
                                 adjT[n, h, :, i * JC:(i + 1) * JC, :]).then_inc(raw_loaded[h][i], 16)

            def load_x(n, h):
                sp.dma_start(x_sb[:, h * TH:(h + 1) * TH, :],
                             x[n, :, h * TH:(h + 1) * TH, :]).then_inc(x_loaded[h], 16)

            def store(b, h):
                sp.wait_ge(out_done, b * H + h + 1)
                sp.dma_start(out[b, :, h * TH:(h + 1) * TH, :],
                             x1[:, h * TH:(h + 1) * TH, :]).then_inc(x1_free[h], 16)

            sp.dma_start(xt_raw[:], xT[0]).then_inc(xt_loaded, 16)
            sp.dma_start(w_raw, w).then_inc(w_loaded, 16)
            load_adj(0, 0)
            sp.dma_start(k_raw, k).then_inc(k_loaded, 16)
            sp.dma_start(bias_sb[:], bias).then_inc(bias_loaded, 16)
            load_x(0, 0)
            sp.wait_ge(xt_lo_done, FT)
            sp.dma_start(xt_raw[:], xT[1]).then_inc(xt_loaded, 16)
            load_adj(0, 1)
            load_x(0, 1)

            def batch(b, more):
                sp.wait_ge(diag_ready, b * H + 1)
                load_adj(b + 1, 0)
                if more:
                    sp.wait_ge(xt_lo_done, b * FT + 2 * FT)
                    sp.dma_start(xt_raw[:], xT[b + 2]).then_inc(xt_loaded, 16)
                for h in range(H):
                    sp.wait_ge(resid0_done, b * (T // 2) + TH // 2 * (h + 1))
                    load_x(b + 1, h)
                sp.wait_ge(diag_ready, b * H + 2)
                load_adj(b + 1, 1)
                for h in range(H):
                    store(b, h)

            with sp.Fori(0, B - 2) as b:
                batch(b, True)
            batch(B - 2, False)
            for h in range(H):
                store(B - 1, h)
            for h in range(H):
                sp.wait_ge(x1_free[h], 16 * (B + 1))

        @block.gpsimd
        def _(pool):
            nc.gpsimd.memset(ident[:], 0.0).then_inc(ident_zero, 1)
            pool.wait_ge(ident_zero, 1)
            nc.gpsimd.affine_select(out=ident[:, 0, :], in_=ident[:, 0, :], compare_op=ALU.not_equal,
                                    fill=1.0, base=0, pattern=[[-1, P]],
                                    channel_multiplier=1).then_inc(ident_done, 1)

        @block.scalar
        def _(act):
            def copy(o, i):
                return nc.scalar.activation(o, i, ACT.Copy)

            def split_adj(n, h, free=None):
                for i in range(CH):
                    act.wait_ge(raw_loaded[h][i], 16 * (n + 1))
                    if i == 0 and free is not None:
                        act.wait_ge(g_done, free)
                    rows = raw[:, h, i * JC:(i + 1) * JC, :].rearrange("p j m -> p (j m)")
                    copy(adj_chunk(a_hi, h, i), rows).then_inc(adj_hi_done, 1)

            def split_xt(n):
                act.wait_ge(xt_loaded, 16 * (n + 1))
                for f in range(FT):
                    copy(xt_hi[:, f, :], xt_raw[:, f, :]).then_inc(xt_hi_done, 1)

            def read_proj0(n, t, bank):
                act.wait_ge(proj0_done, n * T + t + 1)
                copy(p1[:, t, :], ring_b[:, bank, 0:F])
                copy(z_hi[:, t, 0:F], ring_b[:, bank, F:2 * F]).then_inc(z_hi_done, 1)

            def root(b, step, m):
                act.wait_ge(var_ready, b * 4 + step + 1)
                nc.scalar.activation(s[:, 0:m], v[:, 0:m], ACT.Sqrt,
                                     scale=0.25).then_inc(root_done, 1)

            def norm0(b, h):
                act.wait_ge(nb_done, b * 4 + h + 1)
                act.wait_ge(x1_free[h], 16 * (b + 1))

                def round_x1s(q):
                    t = h * TH + q
                    act.wait_ge(x1_done, b * T + t + 1)
                    nc.scalar.activation(x1s_hi[:, t, :], x1[:, t, :], ACT.Copy,
                                         scale=dh[:, h, q:q + 1]).then_inc(x1s_hi_done, 1)

                for q in range(TH):
                    t = h * TH + q
                    nc.scalar.activation(x1[:, t, :], p1[:, t, :], ACT.Identity,
                                         scale=dh[:, h, TH + q:TH + q + 1],
                                         bias=nb[:, q:q + 1]).then_inc(x1_done, 1)
                    if q > 0:
                        round_x1s(q - 1)
                round_x1s(TH - 1)

            def norm1(b, h):
                act.wait_ge(nb_done, b * 4 + H + h + 1)
                for q in range(TH):
                    t = h * TH + q
                    last = nc.scalar.activation(x1[:, t, :], x1[:, t, :], ACT.Identity,
                                                scale=rstd1[:, q:q + 1], bias=nb[:, q:q + 1])
                last.then_inc(out_done, 1)

            def diagonal(b, h):
                act.wait_ge(agg_done, b * T + TH * (h + 1))
                act.wait_ge(diag_ready, b * H + h + 1)
                copy(adj_diagonal(a_hi, h), diag[:, h * TH:(h + 1) * TH, :]).then_inc(diag_hi_done, 1)

            def read_g(b, n, h, f, bank):
                act.wait_ge(g_done, b * 4 + n + 1)
                copy(g_part(True, h, f), ring_b[:, bank, :]).then_inc(g_hi_done, 1)

            def batch(b, more):
                if more:
                    act.wait_ge(agg_done, b * T + 1)
                    split_xt(b + 1)
                root(b, 0, 2 * TH)
                diagonal(b, 0)
                norm0(b, 0)
                if more:
                    read_proj0(b + 1, 0, 0)
                    read_proj0(b + 1, 1, 1)
                root(b, 1, 2 * TH)
                if more:
                    read_proj0(b + 1, 2, 2)
                norm0(b, 1)
                if more:
                    for t in range(3, PL):
                        read_proj0(b + 1, t, t % NB)
                diagonal(b, 1)
                read_g(b, 0, 0, 0, 2)
                read_g(b, 1, 0, 1, 3)
                if more:
                    split_adj(b + 1, 0, b * 4 + 2)
                read_g(b, 2, 1, 0, 0)
                root(b, 2, TH)
                read_g(b, 3, 1, 1, 1)
                if more:
                    for t in range(PL, T):
                        read_proj0(b + 1, t, t % NB)
                    split_adj(b + 1, 1)
                norm1(b, 0)
                root(b, 3, TH)
                norm1(b, 1)

            nc.scalar.preload_act_table(ACT.Sqrt)
            split_xt(0)
            act.wait_ge(w_loaded, 16)
            copy(w_hi[:], w_raw).then_inc(w_hi_done, 1)
            split_adj(0, 0)
            act.wait_ge(k_loaded, 16)
            copy(k_hi[:], k_raw).then_inc(w_hi_done, 1)
            for t in range(T):
                read_proj0(0, t, t % NB)
            split_adj(0, 1)
            with act.Fori(0, B - 1) as b:
                batch(b, True)
            batch(B - 1, False)

        @block.vector
        def _(dve):
            def minus(o, a, hi):
                return nc.vector.tensor_tensor(o, a, hi.bitcast(F32), ALU.subtract)

            def split_adj(n, h, first=0, end=CH):
                for i in range(first, end):
                    dve.wait_ge(adj_hi_done, n * H * CH + h * CH + i + 1)
                    rows = raw[:, h, i * JC:(i + 1) * JC, :].rearrange("p j m -> p (j m)")
                    minus(adj_chunk(a_lo, h, i), rows, adj_chunk(a_hi, h, i)).then_inc(adj_lo_done, 1)

            def add_identity(h):
                flat = raw[:, :, :, :].rearrange("p h j m -> p (h j m)")
                nc.vector.tensor_tensor(diag[:, h * TH:(h + 1) * TH, :], adj_diagonal(flat, h),
                                        ident[:, :, :].to_broadcast([P, TH, P]),
                                        ALU.add).then_inc(diag_ready, 1)

            def split_xt(n):
                for f in range(FT):
                    dve.wait_ge(xt_hi_done, n * FT + f + 1)
                    minus(xt_lo[:, f, :], xt_raw[:, f, :], xt_hi[:, f, :]).then_inc(xt_lo_done, 1)

            def read_proj0(n, t, bank):
                dve.wait_ge(z_hi_done, n * T + t + 1)
                minus(z_lo[:, t, :], ring_b[:, bank, F:2 * F], z_hi[:, t, 0:F]).then_inc(z_lo_done, 1)

            def add_layer0(b, h, pairs=range(0, TH, 2)):
                dve.wait_ge(x_loaded[h], 16 * (b + 1))
                for q in pairs:
                    t = h * TH + q
                    pair = b * (T // 2) + t // 2 + 1
                    bank = t % NB
                    degree = ring_a[:, bank:bank + 2, F:F + 1]
                    dve.wait_ge(agg_done, b * T + t + 2)
                    nc.vector.tensor_scalar(deg_c[:], degree, DEG_EPS, None,
                                            ALU.max).then_inc(deg_clamped, 1)
                    nc.vector.tensor_scalar(v[:, q:q + 2].rearrange("p (q o) -> p q o", o=1), degree,
                                            1.0, None, ALU.add)
                    dve.wait_ge(deg_clamped, pair)
                    nc.vector.reciprocal(rdeg[:], deg_c[:]).then_inc(rdeg_done, 1)
                    dve.wait_ge(rdeg_done, pair)
                    for o in range(2):
                        nc.vector.scalar_tensor_tensor(
                            p1[:, t + o, :], ring_a[:, bank + o, 0:F], rdeg[:, o, :],
                            p1[:, t + o, :], ALU.mult, ALU.add).then_inc(agg_read, 1)
                    dve.wait_ge(agg_read, b * T + t + 2)
                    nc.vector.scalar_tensor_tensor(
                        p1[:, t:t + 2, :], p1[:, t:t + 2, :], 0.0, x_sb[:, t:t + 2, :],
                        ALU.max, ALU.add).then_inc(resid0_done, 1)
                    dve.wait_ge(resid0_done, pair)
                    for o in range(2):
                        last = nc.vector.bn_stats(stats[:, q + o, :], p1[:, t + o, :])
                    if q == TH - 2:
                        last.then_inc(stats_done, 1)

            def add_layer1(b, h):
                for q in range(0, TH, 2):
                    t = h * TH + q
                    for o in range(2):
                        dve.wait_ge(proj1_done, b * T + t + o + 1)
                        nc.vector.scalar_tensor_tensor(
                            u1[:, o, :], ring_a[:, (t + o) % NB, 0:F], dh[:, h, q + o:q + o + 1],
                            bias_sb[:], ALU.mult, ALU.add).then_inc(proj1_read, 1)
                    dve.wait_ge(proj1_read, b * T + t + 2 + T)
                    nc.vector.scalar_tensor_tensor(
                        x1[:, t:t + 2, :], u1[:, :, :], 0.0, x1[:, t:t + 2, :],
                        ALU.max, ALU.add).then_inc(resid1_done, 1)
                    dve.wait_ge(resid1_done, b * (T // 2) + t // 2 + 1)
                    for o in range(2):
                        last = nc.vector.bn_stats(stats[:, q + o, :], x1[:, t + o, :])
                last.then_inc(stats_done, 1)

            def variances(b, step, at):
                n = b * 4 + step + 1
                even_mean, even_cv, odd_mean, odd_cv = (stats[:, :, i] for i in (1, 2, 4, 5))
                dve.wait_ge(stats_done, n)
                nc.vector.tensor_tensor(dmean[:], even_mean, odd_mean, ALU.subtract).then_inc(dmean_done, 1)
                nc.vector.tensor_tensor(smean[:], even_mean, odd_mean, ALU.add)
                nc.vector.scalar_tensor_tensor(cv[:], even_cv, F * LN_EPS, odd_cv, ALU.add, ALU.add)
                dve.wait_ge(dmean_done, n)
                nc.vector.scalar_tensor_tensor(dmean2[:], dmean[:], 0.25, dmean[:],
                                               ALU.mult, ALU.mult).then_inc(dmean2_done, 1)
                dve.wait_ge(dmean2_done, n)
                nc.vector.scalar_tensor_tensor(v[:, at:at + TH], cv[:], 1.0 / F, dmean2[:],
                                               ALU.mult, ALU.add).then_inc(var_ready, 1)

            def inverse_roots(b, step, m, o, std):
                n = b * 4 + step + 1
                dve.wait_ge(root_done, n)
                nc.vector.reciprocal(r[:, 0:m], s[:, 0:m]).then_inc(recip_done, 1)
                dve.wait_ge(recip_done, n)
                nc.vector.scalar_tensor_tensor(c[:, 0:m], v[:, 0:m], 0.25, r[:, 0:m],
                                               ALU.mult, ALU.mult).then_inc(corr_done, 1)
                dve.wait_ge(corr_done, n)
                nc.vector.tensor_tensor(d[:, 0:m], s[:, 0:m], c[:, 0:m], ALU.add).then_inc(sum_done, 1)
                dve.wait_ge(sum_done, n)
                nc.vector.reciprocal(o, d[:, 0:m]).then_inc(rstd_done, 1)
                dve.wait_ge(rstd_done, n)
                nc.vector.scalar_tensor_tensor(nb[:], smean[:], -0.5, std,
                                               ALU.mult, ALU.mult).then_inc(nb_done, 1)

            def lower_x1s(b, h):
                for q in range(TH):
                    t = h * TH + q
                    dve.wait_ge(x1s_hi_done, b * T + t + 1)
                    nc.vector.scalar_tensor_tensor(
                        x1s_lo[:, t, :], x1[:, t, :], dh[:, h, q:q + 1],
                        x1s_hi[:, t, :].bitcast(F32), ALU.mult, ALU.subtract).then_inc(x1s_lo_done, 1)

            def diagonal(b, h):
                dve.wait_ge(diag_hi_done, b * H + h + 1)
                minus(adj_diagonal(a_lo, h), diag[:, h * TH:(h + 1) * TH, :],
                      adj_diagonal(a_hi, h)).then_inc(diag_lo_done, 1)

            def read_g(b, n, h, f, bank):
                dve.wait_ge(g_hi_done, b * 4 + n + 1)
                minus(g_part(False, h, f), ring_b[:, bank, :], g_part(True, h, f)).then_inc(g_read, 1)

            def batch(b, more):
                add_layer0(b, 0)
                variances(b, 0, TH)
                if more:
                    split_xt(b + 1)
                inverse_roots(b, 0, 2 * TH, dh[:, 0, :], dh[:, 0, TH:2 * TH])
                diagonal(b, 0)
                add_layer0(b, 1, [0])
                lower_x1s(b, 0)
                add_layer0(b, 1, [2])
                variances(b, 1, TH)
                if more:
                    read_proj0(b + 1, 0, 0)
                    read_proj0(b + 1, 1, 1)
                inverse_roots(b, 1, 2 * TH, dh[:, 1, :], dh[:, 1, TH:2 * TH])
                if more:
                    read_proj0(b + 1, 2, 2)
                lower_x1s(b, 1)
                if more:
                    for t in range(3, PL):
                        read_proj0(b + 1, t, t % NB)
                add_identity(1)
                diagonal(b, 1)
                read_g(b, 0, 0, 0, 2)
                read_g(b, 1, 0, 1, 3)
                if more:
                    split_adj(b + 1, 0)
                    add_identity(0)
                read_g(b, 2, 1, 0, 0)
                add_layer1(b, 0)
                variances(b, 2, 0)
                inverse_roots(b, 2, TH, rstd1[:], rstd1[:])
                read_g(b, 3, 1, 1, 1)
                if more:
                    for t in range(PL, T):
                        read_proj0(b + 1, t, t % NB)
                add_layer1(b, 1)
                variances(b, 3, 0)
                if more:
                    split_adj(b + 1, 1, 0, 1)
                inverse_roots(b, 3, TH, rstd1[:], rstd1[:])
                if more:
                    split_adj(b + 1, 1, 1)

            nc.vector.memset(ones[:], 1.0).then_inc(ones_done, 1)
            nc.vector.memset(deg_c[:], 0.0).then_inc(g_read, 4)
            nc.vector.memset(rdeg[:], 0.0).then_inc(proj1_read, T)
            nc.vector.memset(stats[:], 0.0).then_inc(x1_free[0], 16)
            nc.vector.memset(nb[:], 0.0).then_inc(x1_free[1], 16)
            dve.wait_ge(ones_done, 1)
            nc.vector.tensor_copy(z_hi[:, :, F:F + 2], ones[:]).then_inc(z_ones_done, 1)
            split_xt(0)
            dve.wait_ge(w_hi_done, 1)
            minus(w_lo[:], w_raw, w_hi[:]).then_inc(w_lo_done, 1)
            dve.wait_ge(ident_done, 1)
            dve.wait_ge(bias_loaded, 16)
            split_adj(0, 0)
            add_identity(0)
            dve.wait_ge(w_hi_done, 2)
            minus(k_lo[:], k_raw, k_hi[:]).then_inc(w_lo_done, 1)
            for t in range(T):
                read_proj0(0, t, t % NB)
            split_adj(0, 1)
            with dve.Fori(0, B - 1) as b:
                batch(b, True)
            batch(B - 1, False)

        @block.tensor
        def _(pe):
            def product(o, parts):
                for i, (lhi, llo, rhi, rlo) in enumerate(parts):
                    last_part = i == len(parts) - 1
                    w_out = o[:, 0:rlo.shape[-1]]
                    nc.tensor.matmul(o, lhi, rhi, start=(i == 0), stop=False)
                    nc.tensor.matmul(w_out, lhi, rlo, start=False, stop=False)
                    last = nc.tensor.matmul(o, llo, rhi, start=False, stop=last_part)
                return last

            def project0(n, t, bank):
                cols = slice(t * P, (t + 1) * P)
                product(ring_b[:, bank, :],
                        [(xt_hi[:, f, cols], xt_lo[:, f, cols], w_hi[:, f, :], w_lo[:, f, :])
                         for f in range(FT)]).then_inc(proj0_done, 1)

            def aggregate(t):
                h, i0 = t // TH, (t % TH) * P
                product(ring_a[:, t % NB, 0:F + 2],
                        [(adj_block(a_hi, h, j, i0, P), adj_block(a_lo, h, j, i0, P),
                          z_hi[:, j, :], z_lo[:, j, :]) for j in range(T)]).then_inc(agg_done, 1)

            def propagate(b, h, f, bank, first):
                pe.wait_ge(diag_lo_done, b * H + h + 1)
                cols = slice(f * P, (f + 1) * P)
                for j in range(T):
                    if first:
                        pe.wait_ge(x1s_lo_done, b * T + j + 1)
                    lhi, llo = x1s_hi[:, j, cols], x1s_lo[:, j, cols]
                    ahi, alo = adj_block(a_hi, h, j, 0, NH), adj_block(a_lo, h, j, 0, NH)
                    nc.tensor.matmul(ring_b[:, bank, :], lhi, ahi, start=(j == 0), stop=False)
                    nc.tensor.matmul(ring_b[:, bank, :], lhi, alo, start=False, stop=False)
                    last = nc.tensor.matmul(ring_b[:, bank, :], llo, ahi, start=False, stop=(j == T - 1))
                last.then_inc(g_done, 1)

            def project1(t):
                h, cols = t // TH, slice((t % TH) * P, (t % TH + 1) * P)
                product(ring_a[:, t % NB, 0:F],
                        [(g_part(True, h, f)[:, cols], g_part(False, h, f)[:, cols],
                          k_hi[:, f, :], k_lo[:, f, :]) for f in range(FT)]).then_inc(proj1_done, 1)

            def batch(b, more):
                pe.wait_ge(z_lo_done, b * T + T)
                for t in range(T):
                    if t % TH == 0:
                        pe.wait_ge(adj_lo_done, b * H * CH + CH * (t // TH + 1))
                    if t < NB:
                        pe.wait_ge(proj1_read, b * T + t + 1 + T - NB)
                    else:
                        pe.wait_ge(agg_read, b * T + t - NB + 1)
                    aggregate(t)
                if more:
                    pe.wait_ge(xt_lo_done, b * FT + 2 * FT)
                    for t in range(PL):
                        if t < NB:
                            pe.wait_ge(g_read, b * 4 + (3 if t == 0 else 4))
                        else:
                            pe.wait_ge(z_lo_done, b * T + T + t - NB + 1)
                        project0(b + 1, t, t % NB)
                    pe.wait_ge(z_lo_done, b * T + T + 3)
                propagate(b, 0, 0, 2, True)
                if more:
                    pe.wait_ge(z_lo_done, b * T + T + 4)
                propagate(b, 0, 1, 3, False)
                if more:
                    pe.wait_ge(z_lo_done, b * T + T + 5)
                else:
                    pe.wait_ge(g_read, b * 4 + 3)
                propagate(b, 1, 0, 0, False)
                pe.wait_ge(g_read, b * 4 + 2 + 4)
                for t in range(TH):
                    pe.wait_ge(agg_read, b * T + TH + t + 1)
                    project1(t)
                if more:
                    pe.wait_ge(z_lo_done, b * T + T + 6)
                else:
                    pe.wait_ge(g_read, b * 4 + 4)
                propagate(b, 1, 1, 1, False)
                if more:
                    for t in range(PL, T):
                        pe.wait_ge(g_read, b * 4 + t - PL + 1 + 4)
                        project0(b + 1, t, t % NB)
                pe.wait_ge(g_read, b * 4 + 4 + 4)
                for t in range(TH, T):
                    pe.wait_ge(proj1_read, b * T + t - TH + 1 + T)
                    project1(t)

            pe.wait_ge(xt_lo_done, FT)
            pe.wait_ge(w_lo_done, 1)
            for t in range(T):
                if t >= NB:
                    pe.wait_ge(z_lo_done, t - NB + 1)
                project0(0, t, t % NB)
            pe.wait_ge(z_ones_done, 1)
            pe.wait_ge(w_lo_done, 2)
            with pe.Fori(0, B - 1) as b:
                batch(b, True)
            batch(B - 1, False)


def kernel(x, adj, L0_gnn_W, L1_gnn_kernel, L1_gnn_bias):
    import numpy as np
    import concourse.bacc as bacc
    from concourse.bass_utils import run_bass_kernel_spmd

    x, adj, w, k, bias = (np.asarray(a) for a in (x, adj, L0_gnn_W, L1_gnn_kernel, L1_gnn_bias))
    arrays = {
        "adjT": adj.reshape(B, H, NH, T, P).transpose(0, 1, 4, 3, 2),
        "x": x.reshape(B, T, P, F).transpose(0, 2, 1, 3),
        "xT": x.reshape(B, N, FT, P).transpose(0, 3, 2, 1),
        "w": w.reshape(F, 2, FT, P).transpose(3, 2, 1, 0).reshape(P, FT, 2 * F),
        "k": k.reshape(FT, P, F).transpose(1, 0, 2),
        "bias": np.broadcast_to(bias, (P, F)),
    }
    arrays = {name: np.ascontiguousarray(a) for name, a in arrays.items()}

    nc = bacc.Bacc("TRN2", target_bir_lowering=False, num_devices=1)
    ins = [nc.dram_tensor(name, a.shape, F32, kind="ExternalInput").ap() for name, a in arrays.items()]
    out = nc.dram_tensor("out", (B, P, T, F), F32, kind="ExternalOutput").ap()
    gnn_two_layers(nc, *ins, out)
    result = run_bass_kernel_spmd(nc, [arrays], core_ids=[0]).results[0]["out"]
    return result.transpose(0, 2, 1, 3).reshape(B, N, F)
```

```python
import concourse.bass as bass
from concourse import mybir
from contextlib import ExitStack

F32 = mybir.dt.float32
F32R = mybir.dt.float32r
ALU = mybir.AluOpType
ACT = mybir.ActivationFunctionType

P = 128
B, N, F = 8, 1024, 256
T = N // P
FT = F // P
H = 2
NH = N // H
TH = T // H
CH = 4
JC = T // CH
NB = 4
PL = 6
DEG_EPS = 1e-6
LN_EPS = 1e-5


def gnn_two_layers(nc, adjT, x, xT, w, k, bias, out):
    ctx = ExitStack()
    with ctx:
        def sb(name, shape, dt=F32):
            return ctx.enter_context(nc.sbuf_tensor(name, shape, dt))

        def sem(name):
            return ctx.enter_context(nc.semaphore(name))

        raw = sb("adj_raw", [P, H, T, NH])
        a_hi = sb("adj_hi", [P, H * T * NH], F32R)
        a_lo = sb("adj_lo", [P, H * T * NH], F32R)
        diag = sb("adj_diag", [P, T, P])
        xt_raw = sb("xt_raw", [P, FT, N])
        xt_hi = sb("xt_hi", [P, FT, N], F32R)
        xt_lo = sb("xt_lo", [P, FT, N], F32R)
        g1_hi = sb("g1_hi", [P, FT, NH], F32R)
        g1_lo = sb("g1_lo", [P, FT, NH], F32R)
        x_sb = sb("x_sb", [P, T, F])
        x1 = sb("x1", [P, T, F])
        x1s_hi = sb("x1s_hi", [P, T, F], F32R)
        x1s_lo = sb("x1s_lo", [P, T, F], F32R)
        p1 = sb("p1", [P, T, F])
        z_hi = sb("z_hi", [P, T, F + 2], F32R)
        z_lo = sb("z_lo", [P, T, F], F32R)
        w_hi = sb("w_hi", [P, FT, 2 * F], F32R)
        w_lo = sb("w_lo", [P, FT, 2 * F], F32R)
        k_hi = sb("k_hi", [P, FT, F], F32R)
        k_lo = sb("k_lo", [P, FT, F], F32R)
        bias_sb = sb("bias_sb", [P, F])
        u1 = sb("u1", [P, 2, F])
        ident = sb("ident", [P, 1, P])
        ones = sb("ones", [P, T, 2])
        deg_c = sb("deg_c", [P, 2, 1])
        rdeg = sb("rdeg", [P, 2, 1])
        stats = sb("stats", [P, TH, 6])
        smean = sb("smean", [P, TH])
        dmean = sb("dmean", [P, TH])
        dmean2 = sb("dmean2", [P, TH])
        cv = sb("cv", [P, TH])
        v = sb("rs_value", [P, 2 * TH])
        s = sb("rs_root", [P, 2 * TH])
        r = sb("rs_recip", [P, 2 * TH])
        c = sb("rs_corr", [P, 2 * TH])
        d = sb("rs_sum", [P, 2 * TH])
        dh = sb("dh", [P, H, 2 * TH])
        rstd1 = sb("rstd1", [P, TH])
        nb = sb("nb", [P, TH])

        w_raw = x1[:, 0:2 * FT, :].rearrange("p (f o) c -> p f (o c)", f=FT)
        k_raw = x1[:, 2 * FT:3 * FT, :]

        ring_a = ctx.enter_context(nc.psum_tensor("ring_a", [P, NB, 512], F32))
        ring_b = ctx.enter_context(nc.psum_tensor("ring_b", [P, NB, 512], F32))

        w_loaded = [sem(f"w_loaded{f}") for f in range(FT)]
        k_loaded, bias_loaded = sem("k_loaded"), sem("bias_loaded")
        xt0_loaded = [sem(f"xt0_loaded{i}") for i in range(FT + 1)]
        xt_loaded = sem("xt_loaded")
        x_loaded = [sem(f"x_loaded{h}") for h in range(H)]
        raw_loaded = [[sem(f"raw_loaded{h}{i}") for i in range(CH)] for h in range(H)]
        x1_free = [sem(f"x1_free{h}") for h in range(H)]
        ident_zero, ident_done, ones_done = sem("ident_zero"), sem("ident_done"), sem("ones_done")
        start_hi_done, start_lo_done = sem("start_hi_done"), sem("start_lo_done")
        k_hi_done, k_lo_done = sem("k_hi_done"), sem("k_lo_done")
        adj_hi_done, adj_lo_done = sem("adj_hi_done"), sem("adj_lo_done")
        diag_ready = sem("diag_ready")
        diag_hi_done, diag_lo_done = sem("diag_hi_done"), sem("diag_lo_done")
        xt_hi_done, xt_lo_done = sem("xt_hi_done"), sem("xt_lo_done")
        z_hi_done, z_lo_done = sem("z_hi_done"), sem("z_lo_done")
        z_ones_done = sem("z_ones_done")
        proj0_done = sem("proj0_done")
        agg_done, agg_read = sem("agg_done"), sem("agg_read")
        deg_clamped, rdeg_done = sem("deg_clamped"), sem("rdeg_done")
        resid0_done = sem("resid0_done")
        stats_done = sem("stats_done")
        dmean_done, dmean2_done = sem("dmean_done"), sem("dmean2_done")
        var_ready = sem("var_ready")
        root_done = sem("root_done")
        recip_done, corr_done, sum_done = sem("recip_done"), sem("corr_done"), sem("sum_done")
        rstd_done, nb_done = sem("rstd_done"), sem("nb_done")
        x1_done = sem("x1_done")
        x1s_hi_done, x1s_lo_done = sem("x1s_hi_done"), sem("x1s_lo_done")
        g_done, g_hi_done = sem("g_done"), sem("g_hi_done")
        g_read = sem("g_read")
        proj1_done = sem("proj1_done")
        proj1_read = sem("proj1_read")
        resid1_done = sem("resid1_done")
        out_done = sem("out_done")
        last_out_done = sem("last_out_done")

        block = ctx.enter_context(nc.Block())

        def adj_block(t, h, j, i0, n):
            at = (h * T + j) * NH + i0
            return t[:, at:at + n]

        def adj_chunk(t, h, i):
            at = (h * T + i * JC) * NH
            return t[:, at:at + JC * NH]

        def adj_diagonal(t, h):
            step = NH + P
            at = h * T * NH + h * TH * NH
            back = 0 if h == 0 else TH * step - TH * NH
            flat = t[:, at - back:at - back + TH * step]
            return flat.rearrange("p (q m) -> p q m", m=step)[:, :, back:back + P]

        def g_part(hi, h, f):
            if h == 0:
                return (xt_hi if hi else xt_lo)[:, f, 0:NH]
            return (g1_hi if hi else g1_lo)[:, f, :]

        @block.sync
        def _(sp):
            def load_adj(n, h):
                for i in range(CH):
                    sp.dma_start(raw[:, h, i * JC:(i + 1) * JC, :],
                                 adjT[n, h, :, i * JC:(i + 1) * JC, :]).then_inc(raw_loaded[h][i], 16)

            def load_x(n, h):
                sp.dma_start(x_sb[:, h * TH:(h + 1) * TH, :],
                             x[n, :, h * TH:(h + 1) * TH, :]).then_inc(x_loaded[h], 16)

            def store(b, h):
                sp.wait_ge(out_done, b * H + h + 1)
                sp.dma_start(out[b, :, h * TH:(h + 1) * TH, :],
                             x1[:, h * TH:(h + 1) * TH, :]).then_inc(x1_free[h], 16)

            for f in range(FT):
                sp.dma_start(w_raw[:, f, :], w[:, f, :]).then_inc(w_loaded[f], 16)
                sp.dma_start(xt_raw[:, f, 0:NH], xT[0, :, f, 0:NH]).then_inc(xt0_loaded[f], 16)
            sp.dma_start(xt_raw[:, :, NH:N], xT[0, :, :, NH:N]).then_inc(xt0_loaded[FT], 16)
            load_adj(0, 0)
            sp.dma_start(k_raw, k).then_inc(k_loaded, 16)
            sp.dma_start(bias_sb[:], bias).then_inc(bias_loaded, 16)
            load_x(0, 0)
            sp.wait_ge(xt_lo_done, FT)
            sp.dma_start(xt_raw[:], xT[1]).then_inc(xt_loaded, 16)
            load_adj(0, 1)
            load_x(0, 1)

            def batch(b, more):
                sp.wait_ge(diag_ready, b * H + 1)
                load_adj(b + 1, 0)
                if more:
                    sp.wait_ge(xt_lo_done, b * FT + 2 * FT)
                    sp.dma_start(xt_raw[:], xT[b + 2]).then_inc(xt_loaded, 16)
                for h in range(H):
                    sp.wait_ge(resid0_done, b * (T // 2) + TH // 2 * (h + 1))
                    load_x(b + 1, h)
                sp.wait_ge(diag_ready, b * H + 2)
                load_adj(b + 1, 1)
                for h in range(H):
                    store(b, h)

            with sp.Fori(0, B - 2) as b:
                batch(b, True)
            batch(B - 2, False)
            store(B - 1, 0)
            sp.wait_ge(last_out_done, 1)
            store(B - 1, 1)
            for h in range(H):
                sp.wait_ge(x1_free[h], 16 * (B + 1))

        @block.gpsimd
        def _(pool):
            nc.gpsimd.memset(ident[:], 0.0).then_inc(ident_zero, 1)
            pool.wait_ge(ident_zero, 1)
            nc.gpsimd.affine_select(out=ident[:, 0, :], in_=ident[:, 0, :], compare_op=ALU.not_equal,
                                    fill=1.0, base=0, pattern=[[-1, P]],
                                    channel_multiplier=1).then_inc(ident_done, 1)

        @block.scalar
        def _(act):
            def copy(o, i):
                return nc.scalar.activation(o, i, ACT.Copy)

            def split_adj(n, h, free=None, chunks=range(CH)):
                for i in chunks:
                    act.wait_ge(raw_loaded[h][i], 16 * (n + 1))
                    if i == 0 and free is not None:
                        act.wait_ge(g_done, free)
                    rows = raw[:, h, i * JC:(i + 1) * JC, :].rearrange("p j m -> p (j m)")
                    copy(adj_chunk(a_hi, h, i), rows).then_inc(adj_hi_done, 1)

            def split_xt(n):
                act.wait_ge(xt_loaded, 16 * n)
                for f in range(FT):
                    copy(xt_hi[:, f, :], xt_raw[:, f, :]).then_inc(xt_hi_done, 1)

            def read_proj0(n, t, bank):
                act.wait_ge(proj0_done, n * T + t + 1)
                copy(p1[:, t, :], ring_b[:, bank, 0:F])
                copy(z_hi[:, t, 0:F], ring_b[:, bank, F:2 * F]).then_inc(z_hi_done, 1)

            def root(b, step, m):
                act.wait_ge(var_ready, b * 4 + step + 1)
                nc.scalar.activation(s[:, 0:m], v[:, 0:m], ACT.Sqrt,
                                     scale=0.25).then_inc(root_done, 1)

            def norm0(b, h):
                act.wait_ge(nb_done, b * 4 + h + 1)
                act.wait_ge(x1_free[h], 16 * (b + 1))

                def round_x1s(q):
                    t = h * TH + q
                    act.wait_ge(x1_done, b * T + t + 1)
                    nc.scalar.activation(x1s_hi[:, t, :], x1[:, t, :], ACT.Copy,
                                         scale=dh[:, h, q:q + 1]).then_inc(x1s_hi_done, 1)

                for q in range(TH):
                    t = h * TH + q
                    nc.scalar.activation(x1[:, t, :], p1[:, t, :], ACT.Identity,
                                         scale=dh[:, h, TH + q:TH + q + 1],
                                         bias=nb[:, q:q + 1]).then_inc(x1_done, 1)
                    if q > 0:
                        round_x1s(q - 1)
                round_x1s(TH - 1)

            def norm1(b, h, tiles=range(TH)):
                act.wait_ge(nb_done, b * 4 + H + h + 1)
                for q in tiles:
                    t = h * TH + q
                    last = nc.scalar.activation(x1[:, t, :], x1[:, t, :], ACT.Identity,
                                                scale=rstd1[:, q:q + 1], bias=nb[:, q:q + 1])
                last.then_inc(out_done, 1)

            def diagonal(b, h):
                act.wait_ge(agg_done, b * T + TH * (h + 1))
                act.wait_ge(diag_ready, b * H + h + 1)
                copy(adj_diagonal(a_hi, h), diag[:, h * TH:(h + 1) * TH, :]).then_inc(diag_hi_done, 1)

            def read_g(b, n, h, f, bank):
                act.wait_ge(g_done, b * 4 + n + 1)
                copy(g_part(True, h, f), ring_b[:, bank, :]).then_inc(g_hi_done, 1)

            def batch(b, more):
                if more:
                    act.wait_ge(agg_done, b * T + 1)
                    split_xt(b + 1)
                root(b, 0, 2 * TH)
                diagonal(b, 0)
                norm0(b, 0)
                if more:
                    read_proj0(b + 1, 0, 0)
                    read_proj0(b + 1, 1, 1)
                root(b, 1, 2 * TH)
                if more:
                    read_proj0(b + 1, 2, 2)
                    read_proj0(b + 1, 3, 3)
                norm0(b, 1)
                if more:
                    for t in range(4, PL):
                        read_proj0(b + 1, t, t % NB)
                diagonal(b, 1)
                read_g(b, 0, 0, 0, 2)
                read_g(b, 1, 0, 1, 3)
                if more:
                    split_adj(b + 1, 0, b * 4 + 2)
                read_g(b, 2, 1, 0, 0)
                if more:
                    root(b, 2, TH)
                read_g(b, 3, 1, 1, 1)
                if not more:
                    root(b, 2, TH)
                if more:
                    for t in range(PL, T):
                        read_proj0(b + 1, t, t % NB)
                    split_adj(b + 1, 1)
                norm1(b, 0)
                root(b, 3, TH)
                norm1(b, 1, range(TH if more else TH // 2))

            nc.scalar.preload_act_table(ACT.Sqrt)
            for f in range(FT):
                act.wait_ge(w_loaded[f], 16)
                copy(w_hi[:, f, :], w_raw[:, f, :]).then_inc(start_hi_done, 1)
                act.wait_ge(xt0_loaded[f], 16)
                copy(xt_hi[:, f, 0:NH], xt_raw[:, f, 0:NH]).then_inc(start_hi_done, 1)
            act.wait_ge(xt0_loaded[FT], 16)
            copy(xt_hi[:, :, NH:N], xt_raw[:, :, NH:N]).then_inc(xt_hi_done, FT)
            for t in range(T):
                read_proj0(0, t, t % NB)
                if t < CH:
                    split_adj(0, 0, chunks=[t])
            act.wait_ge(k_loaded, 16)
            copy(k_hi[:], k_raw).then_inc(k_hi_done, 1)
            split_adj(0, 1)
            with act.Fori(0, B - 1) as b:
                batch(b, True)
            batch(B - 1, False)

        @block.vector
        def _(dve):
            def minus(o, a, hi):
                return nc.vector.tensor_tensor(o, a, hi.bitcast(F32), ALU.subtract)

            def split_adj(n, h, first=0, end=CH):
                for i in range(first, end):
                    dve.wait_ge(adj_hi_done, n * H * CH + h * CH + i + 1)
                    rows = raw[:, h, i * JC:(i + 1) * JC, :].rearrange("p j m -> p (j m)")
                    minus(adj_chunk(a_lo, h, i), rows, adj_chunk(a_hi, h, i)).then_inc(adj_lo_done, 1)

            def add_identity(h):
                flat = raw[:, :, :, :].rearrange("p h j m -> p (h j m)")
                nc.vector.tensor_tensor(diag[:, h * TH:(h + 1) * TH, :], adj_diagonal(flat, h),
                                        ident[:, :, :].to_broadcast([P, TH, P]),
                                        ALU.add).then_inc(diag_ready, 1)

            def split_xt(n):
                for f in range(FT):
                    dve.wait_ge(xt_hi_done, n * FT + f + 1)
                    minus(xt_lo[:, f, :], xt_raw[:, f, :], xt_hi[:, f, :]).then_inc(xt_lo_done, 1)

            def read_proj0(n, t, bank):
                dve.wait_ge(z_hi_done, n * T + t + 1)
                minus(z_lo[:, t, :], ring_b[:, bank, F:2 * F], z_hi[:, t, 0:F]).then_inc(z_lo_done, 1)

            def add_layer0(b, h):
                dve.wait_ge(x_loaded[h], 16 * (b + 1))
                for q in range(0, TH, 2):
                    t = h * TH + q
                    pair = b * (T // 2) + t // 2 + 1
                    bank = t % NB
                    degree = ring_a[:, bank:bank + 2, F:F + 1]
                    dve.wait_ge(agg_done, b * T + t + 2)
                    nc.vector.tensor_scalar(deg_c[:], degree, DEG_EPS, None,
                                            ALU.max).then_inc(deg_clamped, 1)
                    nc.vector.tensor_scalar(v[:, q:q + 2].rearrange("p (q o) -> p q o", o=1), degree,
                                            1.0, None, ALU.add)
                    dve.wait_ge(deg_clamped, pair)
                    nc.vector.reciprocal(rdeg[:], deg_c[:]).then_inc(rdeg_done, 1)
                    dve.wait_ge(rdeg_done, pair)
                    for o in range(2):
                        nc.vector.scalar_tensor_tensor(
                            p1[:, t + o, :], ring_a[:, bank + o, 0:F], rdeg[:, o, :],
                            p1[:, t + o, :], ALU.mult, ALU.add).then_inc(agg_read, 1)
                    dve.wait_ge(agg_read, b * T + t + 2)
                    nc.vector.scalar_tensor_tensor(
                        p1[:, t:t + 2, :], p1[:, t:t + 2, :], 0.0, x_sb[:, t:t + 2, :],
                        ALU.max, ALU.add).then_inc(resid0_done, 1)
                    dve.wait_ge(resid0_done, pair)
                    for o in range(2):
                        last = nc.vector.bn_stats(stats[:, q + o, :], p1[:, t + o, :])
                    if q == TH - 2:
                        last.then_inc(stats_done, 1)

            def add_layer1(b, h):
                for q in range(0, TH, 2):
                    t = h * TH + q
                    for o in range(2):
                        dve.wait_ge(proj1_done, b * T + t + o + 1)
                        nc.vector.scalar_tensor_tensor(
                            u1[:, o, :], ring_a[:, (t + o) % NB, 0:F], dh[:, h, q + o:q + o + 1],
                            bias_sb[:], ALU.mult, ALU.add).then_inc(proj1_read, 1)
                    dve.wait_ge(proj1_read, b * T + t + 2 + T)
                    nc.vector.scalar_tensor_tensor(
                        x1[:, t:t + 2, :], u1[:, :, :], 0.0, x1[:, t:t + 2, :],
                        ALU.max, ALU.add).then_inc(resid1_done, 1)
                    dve.wait_ge(resid1_done, b * (T // 2) + t // 2 + 1)
                    for o in range(2):
                        last = nc.vector.bn_stats(stats[:, q + o, :], x1[:, t + o, :])
                last.then_inc(stats_done, 1)

            def variances(b, step, at):
                n = b * 4 + step + 1
                even_mean, even_cv, odd_mean, odd_cv = (stats[:, :, i] for i in (1, 2, 4, 5))
                dve.wait_ge(stats_done, n)
                nc.vector.tensor_tensor(dmean[:], even_mean, odd_mean, ALU.subtract).then_inc(dmean_done, 1)
                nc.vector.tensor_tensor(smean[:], even_mean, odd_mean, ALU.add)
                nc.vector.scalar_tensor_tensor(cv[:], even_cv, F * LN_EPS, odd_cv, ALU.add, ALU.add)
                dve.wait_ge(dmean_done, n)
                nc.vector.scalar_tensor_tensor(dmean2[:], dmean[:], 0.25, dmean[:],
                                               ALU.mult, ALU.mult).then_inc(dmean2_done, 1)
                dve.wait_ge(dmean2_done, n)
                nc.vector.scalar_tensor_tensor(v[:, at:at + TH], cv[:], 1.0 / F, dmean2[:],
                                               ALU.mult, ALU.add).then_inc(var_ready, 1)

            def inverse_roots(b, step, m, o, std):
                n = b * 4 + step + 1
                dve.wait_ge(root_done, n)
                nc.vector.reciprocal(r[:, 0:m], s[:, 0:m]).then_inc(recip_done, 1)
                dve.wait_ge(recip_done, n)
                nc.vector.scalar_tensor_tensor(c[:, 0:m], v[:, 0:m], 0.25, r[:, 0:m],
                                               ALU.mult, ALU.mult).then_inc(corr_done, 1)
                dve.wait_ge(corr_done, n)
                nc.vector.tensor_tensor(d[:, 0:m], s[:, 0:m], c[:, 0:m], ALU.add).then_inc(sum_done, 1)
                dve.wait_ge(sum_done, n)
                nc.vector.reciprocal(o, d[:, 0:m]).then_inc(rstd_done, 1)
                dve.wait_ge(rstd_done, n)
                nc.vector.scalar_tensor_tensor(nb[:], smean[:], -0.5, std,
                                               ALU.mult, ALU.mult).then_inc(nb_done, 1)

            def lower_x1s(b, h, tiles=range(TH)):
                for q in tiles:
                    t = h * TH + q
                    dve.wait_ge(x1s_hi_done, b * T + t + 1)
                    nc.vector.scalar_tensor_tensor(
                        x1s_lo[:, t, :], x1[:, t, :], dh[:, h, q:q + 1],
                        x1s_hi[:, t, :].bitcast(F32), ALU.mult, ALU.subtract).then_inc(x1s_lo_done, 1)

            def diagonal(b, h):
                dve.wait_ge(diag_hi_done, b * H + h + 1)
                minus(adj_diagonal(a_lo, h), diag[:, h * TH:(h + 1) * TH, :],
                      adj_diagonal(a_hi, h)).then_inc(diag_lo_done, 1)

            def read_g(b, n, h, f, bank):
                dve.wait_ge(g_hi_done, b * 4 + n + 1)
                minus(g_part(False, h, f), ring_b[:, bank, :], g_part(True, h, f)).then_inc(g_read, 1)

            def batch(b, more):
                add_layer0(b, 0)
                variances(b, 0, TH)
                if more:
                    split_xt(b + 1)
                inverse_roots(b, 0, 2 * TH, dh[:, 0, :], dh[:, 0, TH:2 * TH])
                diagonal(b, 0)
                if not more:
                    lower_x1s(b, 0)
                add_layer0(b, 1)
                variances(b, 1, TH)
                if more:
                    read_proj0(b + 1, 0, 0)
                    read_proj0(b + 1, 1, 1)
                    lower_x1s(b, 0, range(0, 2))
                inverse_roots(b, 1, 2 * TH, dh[:, 1, :], dh[:, 1, TH:2 * TH])
                if more:
                    read_proj0(b + 1, 2, 2)
                    lower_x1s(b, 0, range(2, TH))
                    read_proj0(b + 1, 3, 3)
                lower_x1s(b, 1)
                if more:
                    for t in range(4, PL):
                        read_proj0(b + 1, t, t % NB)
                add_identity(1)
                diagonal(b, 1)
                read_g(b, 0, 0, 0, 2)
                read_g(b, 1, 0, 1, 3)
                if more:
                    split_adj(b + 1, 0)
                    add_identity(0)
                read_g(b, 2, 1, 0, 0)
                add_layer1(b, 0)
                if not more:
                    read_g(b, 3, 1, 1, 1)
                variances(b, 2, 0)
                inverse_roots(b, 2, TH, rstd1[:], rstd1[:])
                if more:
                    read_g(b, 3, 1, 1, 1)
                if more:
                    for t in range(PL, T):
                        read_proj0(b + 1, t, t % NB)
                add_layer1(b, 1)
                variances(b, 3, 0)
                if more:
                    split_adj(b + 1, 1, 0, 1)
                inverse_roots(b, 3, TH, rstd1[:], rstd1[:])
                if more:
                    split_adj(b + 1, 1, 1)
                else:
                    dve.wait_ge(nb_done, b * 4 + 4)
                    for q in range(TH // 2, TH):
                        last = nc.vector.tensor_scalar(x1[:, TH + q, :], x1[:, TH + q, :],
                                                       rstd1[:, q:q + 1], nb[:, q:q + 1],
                                                       ALU.mult, ALU.add)
                    last.then_inc(last_out_done, 1)

            nc.vector.memset(ones[:], 1.0).then_inc(ones_done, 1)
            nc.vector.memset(deg_c[:], 0.0).then_inc(g_read, 4)
            nc.vector.memset(rdeg[:], 0.0).then_inc(proj1_read, T)
            nc.vector.memset(stats[:], 0.0).then_inc(x1_free[0], 16)
            nc.vector.memset(nb[:], 0.0).then_inc(x1_free[1], 16)
            dve.wait_ge(ones_done, 1)
            nc.vector.tensor_copy(z_hi[:, :, F:F + 2], ones[:]).then_inc(z_ones_done, 1)
            for f in range(FT):
                dve.wait_ge(start_hi_done, 2 * f + 1)
                minus(w_lo[:, f, :], w_raw[:, f, :], w_hi[:, f, :]).then_inc(start_lo_done, 1)
                dve.wait_ge(start_hi_done, 2 * f + 2)
                minus(xt_lo[:, f, 0:NH], xt_raw[:, f, 0:NH], xt_hi[:, f, 0:NH]).then_inc(start_lo_done, 1)
            dve.wait_ge(xt_hi_done, FT)
            minus(xt_lo[:, :, NH:N], xt_raw[:, :, NH:N], xt_hi[:, :, NH:N]).then_inc(xt_lo_done, FT)
            for t in range(T):
                read_proj0(0, t, t % NB)
                if t < CH:
                    split_adj(0, 0, t, t + 1)
            dve.wait_ge(ident_done, 1)
            add_identity(0)
            dve.wait_ge(k_hi_done, 1)
            minus(k_lo[:], k_raw, k_hi[:]).then_inc(k_lo_done, 1)
            split_adj(0, 1)
            dve.wait_ge(bias_loaded, 16)
            with dve.Fori(0, B - 1) as b:
                batch(b, True)
            batch(B - 1, False)

        @block.tensor
        def _(pe):
            def product(o, parts, first=True, final=True):
                for i, (lhi, llo, rhi, rlo) in enumerate(parts):
                    last_part = final and i == len(parts) - 1
                    narrow = o[:, 0:rlo.shape[-1]]
                    nc.tensor.matmul(o, lhi, rhi, start=(first and i == 0), stop=False)
                    nc.tensor.matmul(narrow, lhi, rlo, start=False, stop=False)
                    last = nc.tensor.matmul(o, llo, rhi, start=False, stop=last_part)
                return last

            def project0(n, t, bank):
                cols = slice(t * P, (t + 1) * P)
                for f in range(FT):
                    if type(n) is int and n == 0 and t == 0:
                        pe.wait_ge(start_lo_done, 2 * f + 2)
                    last = product(ring_b[:, bank, :],
                                   [(xt_hi[:, f, cols], xt_lo[:, f, cols], w_hi[:, f, :], w_lo[:, f, :])],
                                   f == 0, f == FT - 1)
                last.then_inc(proj0_done, 1)

            def aggregate(b, t):
                h, i0 = t // TH, (t % TH) * P
                for j in range(T):
                    if t == 0:
                        pe.wait_ge(z_lo_done, b * T + j + 1)
                    last = product(ring_a[:, t % NB, 0:F + 2],
                                   [(adj_block(a_hi, h, j, i0, P), adj_block(a_lo, h, j, i0, P),
                                     z_hi[:, j, :], z_lo[:, j, :])], j == 0, j == T - 1)
                last.then_inc(agg_done, 1)

            def propagate(h, f, bank, sources):
                cols = slice(f * P, (f + 1) * P)
                for j in sources:
                    lhi, llo = x1s_hi[:, j, cols], x1s_lo[:, j, cols]
                    ahi, alo = adj_block(a_hi, h, j, 0, NH), adj_block(a_lo, h, j, 0, NH)
                    nc.tensor.matmul(ring_b[:, bank, :], lhi, ahi, start=(j == 0), stop=False)
                    nc.tensor.matmul(ring_b[:, bank, :], lhi, alo, start=False, stop=False)
                    last = nc.tensor.matmul(ring_b[:, bank, :], llo, ahi, start=False, stop=(j == T - 1))
                if sources[-1] == T - 1:
                    last.then_inc(g_done, 1)

            def project1(t):
                h, cols = t // TH, slice((t % TH) * P, (t % TH + 1) * P)
                product(ring_a[:, t % NB, 0:F],
                        [(g_part(True, h, f)[:, cols], g_part(False, h, f)[:, cols],
                          k_hi[:, f, :], k_lo[:, f, :]) for f in range(FT)]).then_inc(proj1_done, 1)

            def batch(b, more):
                for t in range(T):
                    if t % TH == 0:
                        pe.wait_ge(adj_lo_done, b * H * CH + CH * (t // TH + 1))
                    if t < NB:
                        pe.wait_ge(proj1_read, b * T + t + 1 + T - NB)
                    else:
                        pe.wait_ge(agg_read, b * T + t - NB + 1)
                    aggregate(b, t)
                if more:
                    pe.wait_ge(xt_lo_done, b * FT + 2 * FT)
                    for t in range(PL):
                        if t < NB:
                            pe.wait_ge(g_read, b * 4 + (3 if t == 0 else 4))
                        else:
                            pe.wait_ge(z_lo_done, b * T + T + t - NB + 1)
                        project0(b + 1, t, t % NB)
                    pe.wait_ge(z_lo_done, b * T + T + 3)
                pe.wait_ge(diag_lo_done, b * H + 1)
                for first in (0, TH):
                    for f in range(FT):
                        if more and first == 0 and f == 1:
                            pe.wait_ge(z_lo_done, b * T + T + 4)
                        for j in range(first, first + TH):
                            if f == 0:
                                pe.wait_ge(x1s_lo_done, b * T + j + 1)
                            propagate(0, f, 2 + f, [j])
                    if first == 0 and not more:
                        for f in range(FT):
                            pe.wait_ge(g_read, b * 4 + 3 + f)
                            propagate(1, f, f, range(TH))
                if more:
                    pe.wait_ge(z_lo_done, b * T + T + 5)
                pe.wait_ge(diag_lo_done, b * H + 2)
                rest = range(0 if more else TH, T)
                propagate(1, 0, 0, rest)
                pe.wait_ge(k_lo_done, 1)
                pe.wait_ge(g_read, b * 4 + 2 + 4)
                for t in range(TH):
                    pe.wait_ge(agg_read, b * T + TH + t + 1)
                    project1(t)
                if more:
                    pe.wait_ge(z_lo_done, b * T + T + 6)
                propagate(1, 1, 1, rest)
                if more:
                    for t in range(PL, T):
                        pe.wait_ge(g_read, b * 4 + t - PL + 1 + 4)
                        project0(b + 1, t, t % NB)
                pe.wait_ge(g_read, b * 4 + 4 + 4)
                for t in range(TH, T):
                    pe.wait_ge(proj1_read, b * T + t - TH + 1 + T)
                    project1(t)

            for t in range(T):
                if t == TH:
                    pe.wait_ge(xt_lo_done, FT)
                if t >= NB:
                    pe.wait_ge(z_lo_done, t - NB + 1)
                project0(0, t, t % NB)
            pe.wait_ge(z_ones_done, 1)
            with pe.Fori(0, B - 1) as b:
                batch(b, True)
            batch(B - 1, False)


def kernel(x, adj, L0_gnn_W, L1_gnn_kernel, L1_gnn_bias):
    import numpy as np
    import concourse.bacc as bacc
    from concourse.bass_utils import run_bass_kernel_spmd

    x, adj, w, k, bias = (np.asarray(a) for a in (x, adj, L0_gnn_W, L1_gnn_kernel, L1_gnn_bias))
    arrays = {
        "adjT": adj.reshape(B, H, NH, T, P).transpose(0, 1, 4, 3, 2),
        "x": x.reshape(B, T, P, F).transpose(0, 2, 1, 3),
        "xT": x.reshape(B, N, FT, P).transpose(0, 3, 2, 1),
        "w": w.reshape(F, 2, FT, P).transpose(3, 2, 1, 0).reshape(P, FT, 2 * F),
        "k": k.reshape(FT, P, F).transpose(1, 0, 2),
        "bias": np.broadcast_to(bias, (P, F)),
    }
    arrays = {name: np.ascontiguousarray(a) for name, a in arrays.items()}

    nc = bacc.Bacc("TRN2", target_bir_lowering=False, num_devices=1)
    ins = [nc.dram_tensor(name, a.shape, F32, kind="ExternalInput").ap() for name, a in arrays.items()]
    out = nc.dram_tensor("out", (B, P, T, F), F32, kind="ExternalOutput").ap()
    gnn_two_layers(nc, *ins, out)
    result = run_bass_kernel_spmd(nc, [arrays], core_ids=[0]).results[0]["out"]
    return result.transpose(0, 2, 1, 3).reshape(B, N, F)
```
